# Optimizing a Trainium2 kernel written in Bass

```python
import numpy as np
import jax
import jax.numpy as jnp

def _softmax(x, axis=-1):
    return jax.nn.softmax(x, axis=axis)

def _gelu(x):
    return jax.nn.gelu(x, approximate=True)

def _silu(x):
    return jax.nn.silu(x)

def _sigmoid(x):
    return jax.nn.sigmoid(x)

def _layernorm(x, axis=-1, eps=1e-05):
    m = jnp.mean(x, axis=axis, keepdims=True)
    v = jnp.var(x, axis=axis, keepdims=True)
    return (x - m) / jnp.sqrt(v + eps)

def _scatter_add(tgt, idx, src, axis=0):
    return tgt.at[idx].add(src)

def _segment_sum(src, seg, n):
    return jax.ops.segment_sum(src, seg, n)
kernel_name = 'mk_adj_resnorm_d2_adj_r2_95c6bc'

def setup_inputs(seed: int=0):
    np.random.seed(seed)
    _w = jnp.asarray

    def _rec_inputs():
        import jax
        import jax.numpy as jnp
        _gk = jax.random.key(seed)
        x = -0.0002928 + 1 * jax.random.normal(jax.random.fold_in(_gk, 1), (2048, 512), jnp.float32)
        _a = jax.random.bernoulli(jax.random.fold_in(_gk, 2), 0.00390625, (2048, 2048))
        _a = jnp.logical_or(_a, jnp.swapaxes(_a, -1, -2))
        _a = jnp.logical_or(_a, jnp.eye(2048, dtype=bool))
        _af = _a.astype(jnp.float32)
        adj = _af
        return (x, adj)
    x, adj = _rec_inputs()

    def _L0_gnn_setup():
        import jax, jax.numpy as jnp
        import numpy as np
        N = 2048
        D_IN = 512
        H = 16
        DH = D_IN // H
        ALPHA = 0.2
        MASK_VAL = -65500.0
        key = jax.random.key(seed)
        ks = jax.random.split(key, 7)
        x = jax.random.normal(ks[0], (N, D_IN), dtype=jnp.float32)
        adj = jax.random.randint(ks[1], (N, N), 0, 2).astype(jnp.float32)
        s = 1.0 / np.sqrt(D_IN)
        W_seq = jax.random.normal(ks[2], (D_IN, D_IN), dtype=jnp.float32) * s
        a1 = jax.random.normal(ks[3], (DH,), dtype=jnp.float32) / np.sqrt(DH)
        a2 = jax.random.normal(ks[4], (DH,), dtype=jnp.float32) / np.sqrt(DH)
        W_out = jax.random.normal(ks[5], (D_IN, D_IN), dtype=jnp.float32) * s
        b_out = jax.random.normal(ks[6], (D_IN,), dtype=jnp.float32) * 0.01
        return {'x': x, 'adj': adj, 'W_seq': W_seq, 'a1': a1, 'a2': a2, 'W_out': W_out, 'b_out': b_out}
    _L0_gnn_all = _L0_gnn_setup()
    _L0_gnn_in = {k: v for k, v in _L0_gnn_all.items() if k in ('W_seq', 'a1', 'a2', 'W_out', 'b_out')}
    del _L0_gnn_all

    def _L1_gnn_setup():
        import jax, jax.numpy as jnp
        import numpy as np
        N = 4096
        D = 512

        def adjacent_mat(adj):
            adj = adj + jnp.eye(adj.shape[0], dtype=adj.dtype)
            deg = jnp.sum(adj, axis=1)
            dinv = jnp.where(deg > 0, deg ** (-0.5), 0.0).astype(adj.dtype)
            return dinv[:, None] * adj * dinv[None, :]
        key = jax.random.key(seed)
        k1, k2 = jax.random.split(key)
        x = jax.random.normal(k1, (N, D), dtype=jnp.float32)
        Coefficient2 = 1e-08 * jnp.ones((N, N), dtype=jnp.float32)
        A = jax.random.uniform(k2, (N, N), dtype=jnp.float32)
        return {'x': x, 'Coefficient2': Coefficient2, 'A': A}
    _L1_gnn_all = _L1_gnn_setup()
    _L1_gnn_in = {k: v for k, v in _L1_gnn_all.items() if k in ()}
    del _L1_gnn_all
    return {'x': x, 'adj': adj, 'L0_gnn_W_seq': _L0_gnn_in['W_seq'], 'L0_gnn_a1': _L0_gnn_in['a1'], 'L0_gnn_a2': _L0_gnn_in['a2'], 'L0_gnn_W_out': _L0_gnn_in['W_out'], 'L0_gnn_b_out': _L0_gnn_in['b_out']}

def reference(x, adj, L0_gnn_W_seq, L0_gnn_a1, L0_gnn_a2, L0_gnn_W_out, L0_gnn_b_out):
    import jax
    import jax.numpy as jnp

    def _L0_gnn_ref(x, adj, W_seq, a1, a2, W_out, b_out):
        import jax, jax.numpy as jnp
        import numpy as np
        N = 2048
        D_IN = 512
        H = 16
        DH = D_IN // H
        ALPHA = 0.2
        MASK_VAL = -65500.0
        seq = (x @ W_seq).reshape(N, H, DH)
        score1 = jnp.einsum('nhd,d->hn', seq, a1)
        score2 = jnp.einsum('nhd,d->hn', seq, a2)
        scores = score1[:, :, None] + score2[:, None, :]
        scores = jax.nn.leaky_relu(scores, negative_slope=ALPHA)
        scores = scores + (1.0 - adj)[None, :, :] * MASK_VAL
        attn = jax.nn.softmax(scores, axis=-1)
        hidden = jnp.einsum('hij,jhd->ihd', attn, seq).reshape(N, D_IN)
        hidden = hidden @ W_out + b_out
        return jax.nn.elu(hidden)

    def _L1_gnn_ref(x, Coefficient2, A):
        import jax, jax.numpy as jnp
        import numpy as np
        N = 4096
        D = 512

        def adjacent_mat(adj):
            adj = adj + jnp.eye(adj.shape[0], dtype=adj.dtype)
            deg = jnp.sum(adj, axis=1)
            dinv = jnp.where(deg > 0, deg ** (-0.5), 0.0).astype(adj.dtype)
            return dinv[:, None] * adj * dinv[None, :]
        A_c = jax.lax.stop_gradient(A)
        adj = adjacent_mat((A_c + A_c.T) * 0.5)
        y = Coefficient2 @ adj
        y = y @ x
        return y
    x = _layernorm(x + _L0_gnn_ref(x, adj, L0_gnn_W_seq, L0_gnn_a1, L0_gnn_a2, L0_gnn_W_out, L0_gnn_b_out), axis=-1)
    x = _layernorm(x + _L1_gnn_ref(x, adj, adj), axis=-1)
    return x

_drawn_inputs = setup_inputs


def setup_inputs(seed=0):
    import zlib

    import numpy as np

    out = dict(_drawn_inputs(seed))
    spreads = {}
    factors = {}
    for name, (base, spread) in spreads.items():
        noise = np.random.default_rng([zlib.crc32(name.encode()), seed]).standard_normal(out[name].shape)
        drawn = base * np.exp(spread * noise) if base else spread * noise
        out[name] = jnp.asarray(drawn.astype(out[name].dtype))
    for name, factor in factors.items():
        out[name] = (out[name] * factor).astype(out[name].dtype)
    return out
```

```python
from contextlib import ExitStack

import concourse.bass as bass
from concourse import mybir

F32 = mybir.dt.float32
F16 = mybir.dt.float16
BF16 = mybir.dt.bfloat16
ALU = mybir.AluOpType
ACT = mybir.ActivationFunctionType
AX = mybir.AxisListType
RMAX = bass.bass_isa.ReduceOp.max

P = 128
N, D, H = 2048, 512, 16
DH = D // H
T = N // P
KC = D // P
ALPHA = 0.2
EPS = 1e-5
STEP = float(2 ** 30)
TOP = float(2 ** 14)
VC = DH + 1
PAIR = 2 * VC
SPLIT = 2 * PAIR
WH = D // 2 + H
GROUP = 2
NG = T // GROUP
SLOTS = 4
T_SCALE = 2.0 ** 8
W_SCALE = 2.0 ** 5
HALF = T // 2
AR = 4

VECTOR_STEPS = (1, 3, 5)
VALUES_AT, LOW_AT, FINISH_AT = 1, 5, (3, 4, 6, 7)
TAKE_AT, HIGH_AT = 2, 4


def bank_of(i):
    return (i // 3, i % 3 * SPLIT) if i < 12 else (4 + (i - 12) // 2, (i - 12) % 2 * SPLIT)


def first_in_bank(i):
    return bank_of(i)[1] == 0


def gat_gcn_kernel(nc, x_d, adj_d, wseq_d, a1_d, a2_d, wout_d, bout_d, out_d):
    ctx = ExitStack()
    with ctx:
        def sb(name, shape, dt):
            return ctx.enter_context(nc.sbuf_tensor(name, shape, dt))

        def sem(name):
            return ctx.enter_context(nc.semaphore(name))

        s1_d = nc.dram_tensor("s1_rows", [H, N], F32, kind="Internal").ap()

        adjT = sb("adjT", [P, T, N], F16)
        hid = sb("hid", [P, T * D], F32)
        seq = sb("seq", [P, T * D], F32)
        area1 = sb("area1", [P, 8192], F32)
        area2 = sb("area2", [P, 10432], F32)
        ident = sb("ident", [P, P], F32)
        ident16 = sb("ident16", [P, P], F16)
        bd = sb("bd", [P, H, T, 2], F32)
        rho = sb("rho", [P, H, T], F32)
        big_s2 = sb("big_s2", [P, H, T], F32)
        rowsum = sb("rowsum", [P, T], F32)
        colsum = sb("colsum", [P, T], F32)
        dinv = sb("dinv", [P, 3, T], F32)
        stat = sb("stat", [P, 2, H], F32)
        gstat = sb("gstat", [P, 2, H], F32)
        mv = sb("mv", [P, T, 2], F32)
        mv_one = sb("mv_one", [P, 2, 2], F32)
        bst = sb("bst", [P, 2, 6], F32)
        tiny = sb("tiny", [P, 2, T], F32)
        std = sb("std", [P, 2], F32)
        rden = sb("rden", [P, T], F32)

        seq_t = seq[:, :].rearrange("p (t n) -> p t n", t=T)
        seq_h = seq[:, :].rearrange("p (t h d) -> p t h d", t=T, h=H)
        hid_h = hid[:, :].rearrange("p (t h d) -> p t h d", t=T, h=H)
        x_in = hid[:, 0:1024].rearrange("p (u n) -> p u n", u=2)
        xT = hid[:, 1024:2048].rearrange("p (u c n) -> p u c n", u=2, c=KC)
        w_all = hid[:, 2048:2048 + KC * 2 * WH].rearrange("p (c e n) -> p c e n", c=KC, e=2)
        s12 = hid[:, 4224:4736].rearrange("p (t e h) -> p t e h", t=T, e=2)
        vmax = hid[:, 4736:4992].rearrange("p (t h) -> p t h", t=T)
        vmin = hid[:, 4992:5248].rearrange("p (t h) -> p t h", t=T)
        q_row = hid[:, 5248:5504].rearrange("p (h t) -> p h t", h=H)
        q_hi = hid[:, 5504:5760].rearrange("p (h t) -> p h t", h=H)
        avec = hid[:, 5760:5824].rearrange("p (e d) -> p e d", e=2)
        wtmp = [hid[:, 5824:7872], area1[:, 6144:8192]]
        a_in = area1[:, 0:4096].rearrange("p (u n) -> p u n", u=2)
        a16 = area1[:, 4096:6144].bitcast(F16).rearrange("p (u n) -> p u n", u=2)
        s1row = area2[0:H, 8320:8320 + N]
        ring = area1[:, :].bitcast(F16).rearrange("p (s k n) -> p s k n", s=SLOTS, k=GROUP)
        ring_bf = area1[:, :].bitcast(BF16).rearrange("p (s k n) -> p s k n", s=SLOTS, k=GROUP)
        s1b = area2[:, 0:4096].rearrange("p (u n) -> p u n", u=2)
        rhs = area2[:, 4096:7264].bitcast(F16).rearrange("p (u t e c) -> p u t e c", u=2, t=T, e=3)
        val = area2[:, 7264:8320].rearrange("p (t e c) -> p t e c", t=T, e=2)
        sums = area2[:, 8320:10432].rearrange("p (t e c) -> p t e c", t=T, e=2)
        wout = seq[:, 0:2048].rearrange("p (c n) -> p c n", c=KC)
        x_res = seq[:, 2048:3072].rearrange("p (u n) -> p u n", u=2)
        bout = seq[:, 3072:3584]
        junk = seq[:, 3584:4608].bitcast(F16)
        h_in = area2[:, 6144:7168].rearrange("p (u n) -> p u n", u=2)
        hT = area2[:, 7168:8192].rearrange("p (u c n) -> p u c n", u=2, c=KC)
        pre = area2[:, 8192:9216].rearrange("p (u n) -> p u n", u=2)
        expm = area2[:, 9216:10240].rearrange("p (u n) -> p u n", u=2)
        rows = area1[:, :].rearrange("p (t n) -> p t n", t=T)
        t_split = hid[:, :].bitcast(F16).rearrange("p (s t n) -> p s t n", s=2, t=T)
        w_split = seq[:, :].bitcast(F16).rearrange("p (s t n) -> p s t n", s=2, t=T)
        a_half = area2[:, 0:4096].rearrange("p (u n) -> p u n", u=AR)
        s_ring = area2[:, 4096:6144].bitcast(F16).rearrange("p (u n) -> p u n", u=AR)

        psum = ctx.enter_context(nc.psum_tensor("psum", [P, 8, 512], F32))
        psum16 = psum[:, :, :].bitcast(F16)

        names = """ident_ready a12_loaded wseq_loaded w_a2 wa_ready x_transposed xT_ready
            a_cast a_transposed adj_evac_v adj_evac_s seq_mm seq_evac s2_stats stats_reduced tables_in
            tables_exp s1_transposed s1_copied s1_stored col_done
            val_ready high_ready low_ready rhs_ready step_s mask_ready pe_group sums_ready bout_loaded wout_loaded
            hid_ready h_copied h_transposed hT_ready proj_done pre_ready exp_done row_ready var_ready std_ready
            t_high t_ready x_norm s_ready w_high w_ready y_ready y_used out_done stored v_chain""".split()
        S = {n: sem(n) for n in names}
        x_loaded = [sem(f"x_loaded{u}") for u in range(2)]
        a_loaded = [sem(f"a_loaded{u}") for u in range(2)]
        s1b_loaded = [sem(f"s1b_loaded{u}") for u in range(2)]
        xr_loaded = [sem(f"xr_loaded{u}") for u in range(2)]
        ah_loaded = [sem(f"ah_loaded{u}") for u in range(AR)]

        x_t = x_d.rearrange("(t p) n -> p t n", p=P)
        adj_t = adj_d.rearrange("(t p) n -> p t n", p=P)
        out_t = out_d.rearrange("(t p) n -> p t n", p=P)

        def w_head(e):
            return w_all[:, :, e, 0:D // 2].rearrange("p c (h d) -> p c h d", d=DH)

        def a_head(a):
            return avec[:, a:a + 1, :].unsqueeze(1).to_broadcast([P, KC, H // 2, DH])

        def fold_view(a, e):
            return wtmp[a].rearrange("p (e c h d) -> p e c h d", e=2, c=KC, d=DH)[:, e]

        block = ctx.enter_context(nc.Block())

        def u_count(h, u):
            return 8 * h + (16 - 8 * u)

        def pass_loops(g):
            return ((HALF * g, True), (HALF * (1 - g), False))

        @block.sync
        def _(sp):
            for c in range(KC):
                sp.dma_start(w_all[:, c, :, 0:D // 2], wseq_d[c * P:(c + 1) * P, :].rearrange("p (e n) -> p e n", e=2)
                             ).then_inc(S["wseq_loaded"], 16)
            for a, d in enumerate((a1_d, a2_d)):
                sp.dma_start(avec[:, a, :], d.rearrange("(o n) -> o n", o=1).to_broadcast([P, DH])
                             ).then_inc(S["a12_loaded"], 16)

            def load(t, u, again):
                if again is not None:
                    sp.wait_ge(S["x_transposed"], again)
                sp.dma_start(x_in[:, u, :], x_t[:, t, :]).then_inc(x_loaded[u], 16)
                if again is not None:
                    sp.wait_ge(S["a_cast"], again)
                sp.dma_start(a_in[:, u, :], adj_t[:, t, :]).then_inc(a_loaded[u], 16)

            for u in range(2):
                load(u, u, None)
            with sp.Fori(1, T // 2) as p:
                for u in range(2):
                    load(2 * p + u, u, 2 * p + u - 1)
            sp.wait_ge(S["s1_copied"], 1)
            sp.dma_start(s1_d, s1row).then_inc(S["s1_stored"], 16)
            sp.wait_ge(S["s1_stored"], 16)

            def spread(h, u):
                sp.dma_start(s1b[:, u, :], s1_d[bass.ds(h, 1), :].to_broadcast([P, N])).then_inc(s1b_loaded[u], 16)

            spread(0, 0)
            spread(1, 1)
            with sp.Fori(1, H // 2) as p:
                for u in range(2):
                    sp.wait_ge(S["mask_ready"], NG * (2 * p + u - 1))
                    spread(2 * p + u, u)
            sp.wait_ge(S["rhs_ready"], H)
            sp.dma_start(wout, wout_d.rearrange("(c p) n -> p c n", p=P)).then_inc(S["wout_loaded"], 16)
            sp.dma_start(bout, bout_d.rearrange("(o n) -> o n", o=1).to_broadcast([P, D])
                         ).then_inc(S["bout_loaded"], 16)
            for u in range(2):
                sp.dma_start(x_res[:, u, :], x_t[:, u, :]).then_inc(xr_loaded[u], 16)
            sp.wait_ge(S["mask_ready"], NG * H)
            for u in range(AR):
                sp.dma_start(a_half[:, u, :], adj_t[:, u, 0:1024]).then_inc(ah_loaded[u], 16)
            with sp.Fori(1, T // 2) as p:
                for u in range(2):
                    sp.wait_ge(S["row_ready"], 2 * p + u - 1)
                    sp.dma_start(x_res[:, u, :], x_t[:, 2 * p + u, :]).then_inc(xr_loaded[u], 16)
            done = AR
            for g in range(2):
                for first, _ in pass_loops(g):
                    skip = 1 if done == AR and g == 0 and first == 0 else 0
                    with sp.Fori(skip, HALF // AR) as p:
                        for u in range(AR):
                            sp.wait_ge(S["s_ready"], AR * p + u + 1 + (done - AR) - AR * skip)
                            sp.dma_start(a_half[:, u, :],
                                         adj_t[:, AR * p + (first + u), 1024 * g:1024 * g + 1024]
                                         ).then_inc(ah_loaded[u], 16)
                    done += HALF - AR * skip
            with sp.Fori(0, T) as t:
                sp.wait_ge(S["out_done"], t + 1)
                sp.dma_start(out_t[:, t, :], rows[:, t, :]).then_inc(S["stored"], 16)
            sp.wait_ge(S["stored"], 16 * T)

        @block.gpsimd
        def _(pool):
            pool.memset(ident[:, :], 0.0).then_inc(S["ident_ready"], 1)
            pool.wait_ge(S["ident_ready"], 1)
            pool.affine_select(out=ident[:, :], in_=ident[:, :], compare_op=ALU.not_equal, fill=1.0,
                               base=0, pattern=[[-1, P]], channel_multiplier=1).then_inc(S["ident_ready"], 1)
            pool.wait_ge(S["ident_ready"], 2)
            pool.tensor_copy(ident16[:, :], ident[:, :]).then_inc(S["ident_ready"], 1)
            pool.wait_ge(S["wseq_loaded"], 16 * KC)
            pool.wait_ge(S["a12_loaded"], 32)
            for e in range(2):
                ins = pool.tensor_tensor(fold_view(1, e), w_head(e), a_head(1), ALU.mult)
            ins.then_inc(S["w_a2"], 1)
            pool.wait_ge(S["s2_stats"], 1)
            pool.partition_all_reduce(gstat[:, :, :].rearrange("p a h -> p (a h)"),
                                      stat[:, :, :].rearrange("p a h -> p (a h)"), P, RMAX
                                      ).then_inc(S["stats_reduced"], 1)

        @block.scalar
        def _(act):
            def cast(t, u, reused, count):
                act.wait_ge(a_loaded[u], 16 * count)
                if reused is not None:
                    act.wait_ge(S["a_transposed"], reused)
                act.activation(a16[:, u, :], a_in[:, u, :], ACT.Copy,
                               accum_out=rowsum[:, bass.ds(t, 1)]).then_inc(S["a_cast"], 1)

            def evacuate(t, u):
                act.wait_ge(S["x_transposed"], t + 1)
                act.activation(xT[:, u, :, :].rearrange("p c n -> p (c n)"), psum[:, 6 + u, :], ACT.Copy
                               ).then_inc(S["xT_ready"], 1)
                act.wait_ge(S["a_transposed"], 2 * t + 2)
                act.activation(adjT[:, 8:16, bass.ts(t, P)],
                               psum16[:, 5, :].rearrange("p (j n) -> p j n", j=8), ACT.Copy
                               ).then_inc(S["adj_evac_s"], 1)

            cast(0, 0, None, 1)
            evacuate(0, 0)
            cast(1, 1, None, 1)
            with act.Fori(0, T // 2 - 1) as p:
                evacuate(2 * p + 1, 1)
                cast(2 * p + 2, 0, 4 * p + 2, p + 2)
                evacuate(2 * p + 2, 0)
                cast(2 * p + 3, 1, 4 * p + 4, p + 2)
            evacuate(T - 1, 1)

            act.wait_ge(S["tables_in"], 1)
            act.activation(bd[:, :, :, 0], q_row, ACT.Exp).then_inc(S["tables_exp"], 1)
            act.activation(bd[:, :, :, 1], q_row, ACT.Exp, scale=ALPHA).then_inc(S["tables_exp"], 1)
            act.activation(rho[:, :, :], q_hi, ACT.Exp, scale=ALPHA - 1.0).then_inc(S["tables_exp"], 1)
            act.wait_ge(S["s1_transposed"], 1)
            act.activation(s1row, psum[0:H, 0:4, :].rearrange("p b n -> p (b n)"), ACT.Copy, scale=-STEP
                           ).then_inc(S["s1_copied"], 1)

            def high(h, u):
                act.wait_ge(S["val_ready"], h + 1)
                if type(h) is not int or h >= 2:
                    act.wait_ge(S["pe_group"], NG * (h - 1))
                act.activation(rhs[:, u, :, 0:3:2, 0:VC], val, ACT.Copy).then_inc(S["high_ready"], 1)

            def steps(h, u, g, fresh=False):
                q = NG * h + g
                if not fresh:
                    act.wait_ge(S["pe_group"], q - SLOTS + 1)
                if g == 0:
                    act.wait_ge(s1b_loaded[u], u_count(h, u))
                for k in range(1 if g in VECTOR_STEPS else 2):
                    j = GROUP * g + k
                    ins = act.activation(ring_bf[:, g % SLOTS, k, :], s1b[:, u, :], ACT.Relu,
                                         bias=big_s2[:, h, j:j + 1], scale=-1.0)
                ins.then_inc(S["step_s"], 1)

            def take_sums(h):
                act.wait_ge(S["pe_group"], NG * (h + 1))
                if type(h) is not int or h > 0:
                    act.wait_ge(S["hid_ready"], h)
                act.activation(sums[:, 0:12, :, :].rearrange("p (b k) e c -> p b (k e c)", b=4),
                               psum[:, 0:4, 0:3 * SPLIT], ACT.Copy).then_inc(S["sums_ready"], 1)
                act.activation(sums[:, 12:16, :, :].rearrange("p (b k) e c -> p b (k e c)", b=2),
                               psum[:, 4:6, 0:2 * SPLIT], ACT.Copy).then_inc(S["sums_ready"], 1)

            high(0, 0)
            act.wait_ge(S["a_transposed"], 2 * T)
            for g in range(NG):
                steps(0, 0, g, fresh=g < SLOTS)
                if g == HIGH_AT:
                    high(1, 1)
            with act.Fori(0, H // 2 - 1) as p:
                for h, u in ((2 * p + 1, 1), (2 * p + 2, 0)):
                    for g in range(NG):
                        steps(h, u, g)
                        if g == TAKE_AT:
                            take_sums(h - 1)
                        if g == HIGH_AT:
                            high(h + 1, 1 - u)
            for g in range(NG):
                steps(H - 1, 1, g)
                if g == TAKE_AT:
                    take_sums(H - 2)
            take_sums(H - 1)

            def copy_h(t, u):
                if type(t) is not int or t >= 2:
                    act.wait_ge(S["h_transposed"], t - 1)
                act.activation(h_in[:, u, :], hid[:, bass.ts(t, D)], ACT.Copy).then_inc(S["h_copied"], 1)

            def copy_hT(t, u):
                act.wait_ge(S["h_transposed"], t + 1)
                if type(t) is not int or t >= 2:
                    act.wait_ge(S["proj_done"], t - 1)
                act.activation(hT[:, u, :, :].rearrange("p c n -> p (c n)"), psum[:, 6 + u, :], ACT.Copy
                               ).then_inc(S["hT_ready"], 1)

            def exp_t(t, u):
                act.wait_ge(S["pre_ready"], t + 1)
                act.activation(expm[:, u, :], expm[:, u, :], ACT.Exp).then_inc(S["exp_done"], 1)

            def column_sum(t):
                if type(t) is not int or t > 0:
                    act.wait_ge(S["col_done"], t)
                act.activation(junk, adjT[:, t, :], ACT.Copy, accum_out=colsum[:, bass.ds(t, 1)]
                               ).then_inc(S["col_done"], 1)

            act.wait_ge(S["rhs_ready"], H)
            column_sum(0)
            act.wait_ge(S["hid_ready"], H)
            copy_h(0, 0)
            copy_h(1, 1)
            copy_hT(0, 0)
            with act.Fori(0, T // 2 - 1) as p:
                copy_hT(2 * p + 1, 1)
                copy_h(2 * p + 2, 0)
                exp_t(2 * p, 0)
                column_sum(2 * p + 1)
                copy_hT(2 * p + 2, 0)
                copy_h(2 * p + 3, 1)
                exp_t(2 * p + 1, 1)
                column_sum(2 * p + 2)
            copy_hT(T - 1, 1)
            exp_t(T - 2, 0)
            column_sum(T - 1)
            exp_t(T - 1, 1)
            act.wait_ge(S["var_ready"], 1)
            act.activation(tiny[:, :, :], tiny[:, :, :], ACT.Sqrt).then_inc(S["std_ready"], 1)
            with act.Fori(0, T) as t:
                act.wait_ge(S["x_norm"], t + 1)
                act.activation(t_split[:, 0, t, :], rows[:, t, :], ACT.Copy,
                               scale=dinv[:, 1, bass.ds(t, 1)]).then_inc(S["t_high"], 1)
            for g in range(2):
                act.wait_ge(S["pe_group"], NG * H + T * (g + 1))
                for b in range(HALF):
                    i = HALF * g + b
                    act.activation(w_split[:, 0, i, :], psum[:, b, :], ACT.Copy,
                                   scale=dinv[:, 2, i:i + 1]).then_inc(S["w_high"], 1)
            with act.Fori(0, T // 2) as p:
                for u in range(2):
                    act.wait_ge(S["var_ready"], 2 * p + u + 2)
                    act.activation(std[:, u:u + 1], std[:, u:u + 1], ACT.Sqrt).then_inc(S["std_ready"], 1)

        @block.vector
        def _(dve):
            links = [0]

            def link(ins, base=0):
                links[0] += 1
                ins.then_inc(S["v_chain"], 1)
                dve.wait_ge(S["v_chain"], base + links[0])

            dve.wait_ge(S["wseq_loaded"], 16 * KC)
            dve.wait_ge(S["a12_loaded"], 32)
            dve.tensor_tensor(fold_view(0, 0), w_head(0), a_head(0), ALU.mult)
            link(dve.tensor_tensor(fold_view(0, 1), w_head(1), a_head(0), ALU.mult))
            for a in range(2):
                if a:
                    dve.wait_ge(S["w_a2"], 1)
                for e in range(2):
                    ins = dve.reduce_sum(w_all[:, :, a, D // 2 + e * H // 2:D // 2 + (e + 1) * H // 2],
                                         fold_view(a, e), axis=AX.X)
            ins.then_inc(S["wa_ready"], 1)

            def first_layer(t, u):
                dve.wait_ge(S["a_transposed"], 2 * t + 1)
                dve.tensor_copy(adjT[:, 0:8, bass.ts(t, P)],
                                psum16[:, 4, :].rearrange("p (j n) -> p j n", j=8)).then_inc(S["adj_evac_v"], 1)
                dve.wait_ge(S["seq_mm"], t + 1)
                banks = psum[:, 2 * u:2 * u + 2, :]
                dve.tensor_copy(s12[:, t, :, :], banks[:, :, D // 2:WH])
                for extreme, op in ((vmax, ALU.max), (vmin, ALU.min)):
                    dve.tensor_reduce(extreme[:, t, :].rearrange("p (e h) -> p e h", e=2),
                                      banks[:, :, 0:D // 2].rearrange("p e (h d) -> p e h d", d=DH),
                                      axis=AX.X, op=op)
                dve.tensor_copy(seq_t[:, t, :].rearrange("p (e n) -> p e n", e=2), banks[:, :, 0:D // 2]
                                ).then_inc(S["seq_evac"], 1)

            with dve.Fori(0, T // 2) as p:
                for u in range(2):
                    first_layer(2 * p + u, u)

            dve.wait_ge(S["seq_evac"], T)
            s1 = s12[:, :, 0, :].rearrange("p t h -> p h t")
            s2 = s12[:, :, 1, :].rearrange("p t h -> p h t")
            dve.reduce_max(stat[:, 0, :], s2, axis=AX.X)
            dve.reduce_max(stat[:, 1, :], vmax.rearrange("p t h -> p h t"), axis=AX.X)
            link(dve.tensor_reduce(gstat[:, 0, :], vmin.rearrange("p t h -> p h t"), axis=AX.X, op=ALU.min))
            dve.scalar_tensor_tensor(stat[:, 1, :], gstat[:, 0, :], -1.0, stat[:, 1, :], ALU.mult, ALU.max
                                     ).then_inc(S["s2_stats"], 1)
            dve.tensor_scalar(big_s2[:, :, :], s2, STEP, None, ALU.mult)
            dve.wait_ge(S["stats_reduced"], 1)
            m2 = gstat[:, 0, :].unsqueeze(2).to_broadcast([P, H, T])
            dve.tensor_tensor(q_row, s2, m2, ALU.subtract)
            link(dve.tensor_tensor(q_hi, s1, m2, ALU.add))
            link(dve.tensor_scalar(gstat[:, 1, :], gstat[:, 1, :], 1.0, None, ALU.max))
            dve.tensor_scalar(q_hi, q_hi, 0.0, None, ALU.max).then_inc(S["tables_in"], 1)
            link(dve.reciprocal(gstat[:, 1, :], gstat[:, 1, :]))
            link(dve.tensor_scalar(gstat[:, 1, :], gstat[:, 1, :], TOP, None, ALU.mult))
            dve.wait_ge(S["tables_exp"], 2)
            link(dve.tensor_tensor(bd[:, :, :, :].rearrange("p h t e -> p h (t e)"),
                                   bd[:, :, :, :].rearrange("p h t e -> p h (t e)"),
                                   gstat[:, 1, :].unsqueeze(2).to_broadcast([P, H, 2 * T]), ALU.mult))
            n0 = links[0]

            def values(h):
                dve.tensor_copy(val[:, :, :, DH], bd[:, h, :, :])
                dve.tensor_tensor(val[:, :, :, 0:DH], seq_h[:, :, h, :].unsqueeze(2).to_broadcast([P, T, 2, DH]),
                                  bd[:, h, :, :].unsqueeze(3).to_broadcast([P, T, 2, DH]), ALU.mult
                                  ).then_inc(S["val_ready"], 1)

            def low(h, u):
                dve.wait_ge(S["val_ready"], h + 1)
                dve.wait_ge(S["high_ready"], h + 1)
                dve.tensor_tensor(rhs[:, u, :, 0:3:2, VC:PAIR], val, rhs[:, u, :, 0:3:2, 0:VC], ALU.subtract
                                  ).then_inc(S["low_ready"], 1)
                dve.wait_ge(S["low_ready"], h + 1)
                dve.tensor_scalar(rhs[:, u, :, 1, :], rhs[:, u, :, 2, :], -1.0, None, ALU.mult
                                  ).then_inc(S["rhs_ready"], 1)

            def masks(h, u, g, fresh=False):
                q = NG * h + g
                k = 2
                if g in VECTOR_STEPS:
                    k = 1
                    j = GROUP * g + 1
                    if not fresh:
                        dve.wait_ge(S["pe_group"], q - SLOTS + 1)
                    dve.wait_ge(s1b_loaded[u], u_count(h, u))
                    dve.scalar_tensor_tensor(ring[:, g % SLOTS, 1, :], s1b[:, u, :], big_s2[:, h, j:j + 1],
                                             adjT[:, j, :], ALU.is_lt, ALU.mult)
                j = GROUP * g
                dve.wait_ge(S["step_s"], q + 1)
                dve.tensor_tensor(ring[:, g % SLOTS, 0:k, :], ring_bf[:, g % SLOTS, 0:k, :], adjT[:, j:j + k, :],
                                  ALU.min).then_inc(S["mask_ready"], 1)

            V = S["v_chain"]

            def finish(h, part, base):
                if part == 0:
                    dve.wait_ge(S["sums_ready"], 2 * h + 2)
                    dve.tensor_tensor(sums[:, :, :, 0:VC], sums[:, :, :, 0:VC], sums[:, :, :, VC:PAIR], ALU.add
                                      ).then_inc(V, 1)
                elif part == 1:
                    dve.wait_ge(V, base + 1)
                    dve.tensor_tensor(sums[:, :, 1, 0:VC], sums[:, :, 1, 0:VC],
                                      rho[:, h, :].unsqueeze(2).to_broadcast([P, T, VC]), ALU.mult
                                      ).then_inc(V, 1)
                elif part == 2:
                    dve.wait_ge(V, base + 2)
                    dve.tensor_tensor(sums[:, :, 0, 0:VC], sums[:, :, 0, 0:VC], sums[:, :, 1, 0:VC], ALU.add
                                      ).then_inc(V, 1)
                else:
                    dve.wait_ge(V, base + 3)
                    dve.reciprocal(rden[:, :], sums[:, :, 0, DH]).then_inc(V, 1)
                    dve.wait_ge(V, base + 4)
                    dve.tensor_tensor(hid_h[:, :, h, :], sums[:, :, 0, 0:DH],
                                      rden[:, :].unsqueeze(2).to_broadcast([P, T, DH]), ALU.mult
                                      ).then_inc(S["hid_ready"], 1)

            def between(h, u, g, last=False):
                if g == VALUES_AT and not last:
                    values(h + 1)
                if g == LOW_AT and not last:
                    low(h + 1, 1 - u)
                if g in FINISH_AT and not (type(h) is int and h == 0):
                    finish(h - 1, FINISH_AT.index(g), n0 + 4 * (h - 1))

            dve.wait_ge(S["tables_exp"], 3)
            values(0)
            low(0, 0)
            for g in range(NG):
                masks(0, 0, g, fresh=g < SLOTS)
                between(0, 0, g)
            with dve.Fori(0, H // 2 - 1) as p:
                for h, u in ((2 * p + 1, 1), (2 * p + 2, 0)):
                    for g in range(NG):
                        masks(h, u, g)
                        between(h, u, g)
            for g in range(NG):
                masks(H - 1, 1, g)
                between(H - 1, 1, g, last=True)
            for part in range(4):
                finish(H - 1, part, n0 + 4 * (H - 1))
            base = n0 + 4 * H

            def elu_in(t, u, base):
                dve.wait_ge(S["proj_done"], t + 1)
                dve.tensor_tensor(pre[:, u, :], psum[:, u, :], bout, ALU.add).then_inc(V, 1)
                dve.wait_ge(V, base + 1)
                dve.tensor_scalar(expm[:, u, :], pre[:, u, :], 0.0, None, ALU.min).then_inc(S["pre_ready"], 1)

            def elu_out(t, u, count, base):
                dve.wait_ge(S["exp_done"], t + 1)
                dve.scalar_tensor_tensor(pre[:, u, :], pre[:, u, :], 0.0, expm[:, u, :], ALU.max, ALU.add
                                         ).then_inc(V, 1)
                dve.wait_ge(V, base + 1)
                dve.wait_ge(xr_loaded[u], count)
                dve.scalar_tensor_tensor(pre[:, u, :], pre[:, u, :], -1.0, x_res[:, u, :], ALU.add, ALU.add
                                         ).then_inc(S["row_ready"], 1)
                dve.wait_ge(S["row_ready"], t + 1)
                dve.bn_stats(bst[:, u, :], pre[:, u, :]).then_inc(V, 1)
                dve.wait_ge(V, base + 2)
                dve.tensor_scalar(rows[:, t, :], pre[:, u, :], 1.0, None, ALU.mult)
                dve.bn_aggr(mv_one[:, u, :], bst[:, u, :]).then_inc(V, 1)
                dve.wait_ge(V, base + 3)
                dve.tensor_scalar(mv[:, t, :], mv_one[:, u, :], 1.0, None, ALU.mult).then_inc(V, 1)

            dve.wait_ge(S["bout_loaded"], 16)
            dve.wait_ge(S["hid_ready"], H)
            elu_in(0, 0, base)
            with dve.Fori(0, T // 2 - 1) as p:
                for u in range(2):
                    elu_in(2 * p + (u + 1), 1 - u, base + 1 + 5 * (2 * p + u))
                    elu_out(2 * p + u, u, 16 * p + 16, base + 2 + 5 * (2 * p + u))
            elu_in(T - 1, 1, base + 1 + 5 * (T - 2))
            elu_out(T - 2, 0, 8 * T, base + 2 + 5 * (T - 2))
            elu_out(T - 1, 1, 8 * T, base + 1 + 5 * (T - 1))
            links[0] = base + 5 * T
            dve.wait_ge(V, links[0])
            dve.wait_ge(S["col_done"], T)
            dve.tensor_scalar(tiny[:, 0, :], mv[:, :, 1], EPS, None, ALU.add)
            link(dve.tensor_tensor(dinv[:, 0, :], rowsum[:, :], colsum[:, :], ALU.add))
            link(dve.tensor_scalar(dinv[:, 0, :], dinv[:, 0, :], 0.5, 1.0, ALU.mult, ALU.add))
            dve.tensor_scalar(dinv[:, 1, :], dinv[:, 0, :], 0.0, None, ALU.is_gt)
            dve.tensor_scalar(tiny[:, 1, :], dinv[:, 0, :], 1e-30, None, ALU.max).then_inc(S["var_ready"], 1)
            dve.wait_ge(S["std_ready"], 1)
            link(dve.reciprocal(tiny[:, :, :], tiny[:, :, :]))
            dve.tensor_copy(mv[:, :, 1], tiny[:, 0, :])
            link(dve.tensor_tensor(dinv[:, 0, :], tiny[:, 1, :], dinv[:, 1, :], ALU.mult))
            dve.tensor_scalar(dinv[:, 1, :], dinv[:, 0, :], T_SCALE, None, ALU.mult)
            link(dve.tensor_scalar(dinv[:, 2, :], dinv[:, 0, :], 0.5 * W_SCALE / T_SCALE, None, ALU.mult))
            def norm(t):
                dve.tensor_scalar(rows[:, t, :], rows[:, t, :], mv[:, t, 0:1], mv[:, t, 1:2],
                                  ALU.subtract, ALU.mult).then_inc(S["x_norm"], 1)

            def t_low(t):
                dve.wait_ge(S["x_norm"], t + 1)
                dve.wait_ge(S["t_high"], t + 1)
                dve.scalar_tensor_tensor(t_split[:, 1, t, :], rows[:, t, :], dinv[:, 1, bass.ds(t, 1)],
                                         t_split[:, 0, t, :], ALU.mult, ALU.subtract).then_inc(S["t_ready"], 1)

            def s_tile(g, jt, n, u, diagonal, count):
                dve.wait_ge(ah_loaded[u], count)
                if type(n) is not int or n >= AR:
                    dve.wait_ge(S["pe_group"], NG * H + n - AR + 1)
                ins = dve.tensor_tensor(s_ring[:, u, :], a_half[:, u, :],
                                        adjT[:, jt, 1024 * g:1024 * g + 1024], ALU.add)
                if diagonal:
                    ins.then_inc(V, 1)
                    dve.wait_ge(V, links[0] + 1 + (n if g == 0 else n - T + HALF))
                    spot = s_ring[:, u, bass.ds((jt - HALF * g) * P, P)]
                    ins = dve.scalar_tensor_tensor(spot, ident[:, :], 2.0, spot, ALU.mult, ALU.add)
                ins.then_inc(S["s_ready"], 1)

            dve.wait_ge(S["h_transposed"], T)
            dve.wait_ge(S["proj_done"], T)
            n = 0
            for g in range(2):
                for first, diagonal in pass_loops(g):
                    with dve.Fori(0, HALF // AR) as p:
                        for u in range(AR):
                            t = AR * p + (first + u)
                            if g == 0:
                                norm(t)
                            s_tile(g, t, AR * p + (n + u), u, diagonal, 16 * p + (16 * (n // AR) + 16))
                            if g == 0:
                                t_low(t)
                    n += HALF
                dve.wait_ge(S["pe_group"], NG * H + T * (g + 1))
                for b in range(HALF):
                    i = HALF * g + b
                    dve.wait_ge(S["w_high"], i + 1)
                    dve.scalar_tensor_tensor(w_split[:, 1, i, :], psum[:, b, :], dinv[:, 2, i:i + 1],
                                             w_split[:, 0, i, :], ALU.mult, ALU.subtract
                                             ).then_inc(S["w_ready"], 1)
            links[0] += T
            base = links[0]

            def last_norm(t, u, base):
                dve.wait_ge(S["y_ready"], t + 1)
                dve.scalar_tensor_tensor(pre[:, u, :], psum[:, u, :], 1.0 / W_SCALE, rows[:, t, :],
                                         ALU.mult, ALU.add).then_inc(S["y_used"], 1)
                dve.wait_ge(S["y_used"], t + 1)
                dve.bn_stats(bst[:, u, :], pre[:, u, :]).then_inc(V, 1)
                dve.wait_ge(V, base + 1)
                dve.memset(std[:, u:u + 1], EPS)
                dve.bn_aggr(mv_one[:, u, :], bst[:, u, :]).then_inc(V, 1)
                dve.wait_ge(V, base + 2)
                dve.tensor_tensor(std[:, u:u + 1], mv_one[:, u, 1:2], std[:, u:u + 1], ALU.add
                                  ).then_inc(S["var_ready"], 1)
                dve.wait_ge(S["std_ready"], t + 2)
                dve.reciprocal(std[:, u:u + 1], std[:, u:u + 1]).then_inc(V, 1)
                dve.wait_ge(V, base + 3)
                dve.tensor_scalar(rows[:, t, :], pre[:, u, :], mv_one[:, u, 0:1], std[:, u:u + 1],
                                  ALU.subtract, ALU.mult).then_inc(S["out_done"], 1)

            with dve.Fori(0, T // 2) as p:
                for u in range(2):
                    last_norm(2 * p + u, u, base + 3 * (2 * p + u))

        @block.tensor
        def _(pe):
            pe.wait_ge(S["ident_ready"], 3)

            def turn_adj(t, u, reused):
                pe.wait_ge(S["a_cast"], t + 1)
                for half in range(2):
                    if reused:
                        pe.wait_ge(S["adj_evac_s" if half else "adj_evac_v"], t)
                    for b in range(8):
                        ins = pe.transpose(psum16[:, 4 + half, b * P:(b + 1) * P],
                                           a16[:, u, (8 * half + b) * P:(8 * half + b + 1) * P], ident16[:, :])
                    ins.then_inc(S["a_transposed"], 1)

            def project(t, u, count, reused):
                pe.wait_ge(x_loaded[u], count)
                for c in range(KC):
                    ins = pe.transpose(psum[:, 6 + u, c * P:(c + 1) * P], x_in[:, u, c * P:(c + 1) * P], ident[:, :])
                ins.then_inc(S["x_transposed"], 1)
                turn_adj(t, u, reused)
                pe.wait_ge(S["xT_ready"], t + 1)
                if not reused:
                    pe.wait_ge(S["wa_ready"], 1)
                if reused:
                    pe.wait_ge(S["seq_evac"], t - 1 if type(t) is not int else max(t - 1, 1))
                for e in range(2):
                    for c in range(KC):
                        ins = pe.matmul(psum[:, 2 * u + e, 0:WH], xT[:, u, c, :], w_all[:, c, e, :],
                                        start=c == 0, stop=c == KC - 1)
                ins.then_inc(S["seq_mm"], 1)

            project(0, 0, 16, False)
            with pe.Fori(0, T // 2 - 1) as p:
                project(2 * p + 1, 1, 16 * p + 16, True)
                project(2 * p + 2, 0, 16 * p + 32, True)
            project(T - 1, 1, 8 * T, True)

            pe.wait_ge(S["seq_evac"], T)
            pe.wait_ge(S["adj_evac_v"], T)
            pe.wait_ge(S["adj_evac_s"], T)
            for t in range(T):
                ins = pe.transpose(psum[0:H, t // 4, t % 4 * P:(t % 4 + 1) * P], s12[:, t, 0, :], ident[:, :])
            ins.then_inc(S["s1_transposed"], 1)

            def head_group(h, u, g, reused):
                for k in range(GROUP):
                    j = GROUP * g + k
                    for i in range(T):
                        bank, col = bank_of(i)
                        if g == 0 and k == 0 and i in (0, 12) and reused is not None:
                            pe.wait_ge(S["sums_ready"], reused + (i == 12))
                        pe.matmul(psum[:, bank, col + PAIR:col + SPLIT], adjT[:, j, i * P:(i + 1) * P],
                                  rhs[:, u, j, 2, :], start=g == 0 and k == 0 and first_in_bank(i),
                                  stop=True, skip_group_check=True)
                pe.wait_ge(S["mask_ready"], NG * h + g + 1)
                for k in range(GROUP):
                    j = GROUP * g + k
                    for i in range(T):
                        bank, col = bank_of(i)
                        ins = pe.matmul(psum[:, bank, col:col + SPLIT], ring[:, g % SLOTS, k, i * P:(i + 1) * P],
                                        rhs[:, u, j, 0:2, :].rearrange("p e c -> p (e c)"), start=False,
                                        stop=True, skip_group_check=True)
                ins.then_inc(S["pe_group"], 1)

            def head(h, u, reused):
                pe.wait_ge(S["rhs_ready"], h + 1)
                for g in range(NG):
                    head_group(h, u, g, reused)

            pe.wait_ge(S["s1_copied"], 1)
            head(0, 0, None)
            with pe.Fori(0, H // 2 - 1) as p:
                head(2 * p + 1, 1, 4 * p + 1)
                head(2 * p + 2, 0, 4 * p + 3)
            head(H - 1, 1, 2 * (H - 1) - 1)

            def turn_h(t, u, reused):
                pe.wait_ge(S["h_copied"], t + 1)
                if reused is not None:
                    pe.wait_ge(S["hT_ready"], reused)
                for c in range(KC):
                    ins = pe.transpose(psum[:, 6 + u, c * P:(c + 1) * P], h_in[:, u, c * P:(c + 1) * P], ident[:, :])
                ins.then_inc(S["h_transposed"], 1)

            def project_h(t, u, reused):
                pe.wait_ge(S["hT_ready"], t + 1)
                if reused is not None:
                    pe.wait_ge(S["pre_ready"], reused)
                for c in range(KC):
                    ins = pe.matmul(psum[:, u, :], hT[:, u, c, :], wout[:, c, :], start=c == 0, stop=c == KC - 1)
                ins.then_inc(S["proj_done"], 1)

            pe.wait_ge(S["wout_loaded"], 16)
            pe.wait_ge(S["sums_ready"], 2 * H)
            turn_h(0, 0, None)
            turn_h(1, 1, None)
            project_h(0, 0, None)
            turn_h(2, 0, 1)
            project_h(1, 1, None)
            with pe.Fori(1, T // 2 - 1) as p:
                turn_h(2 * p + 1, 1, 2 * p)
                project_h(2 * p, 0, 2 * p - 1)
                turn_h(2 * p + 2, 0, 2 * p + 1)
                project_h(2 * p + 1, 1, 2 * p)
            turn_h(T - 1, 1, T - 2)
            project_h(T - 2, 0, T - 3)
            project_h(T - 1, 1, T - 2)

            def s_step(jt, n, u, first):
                pe.wait_ge(S["t_ready"], jt + 1)
                pe.wait_ge(S["s_ready"], n + 1)
                for b in range(HALF):
                    for s in range(2):
                        ins = pe.matmul(psum[:, b, :], s_ring[:, u, b * P:(b + 1) * P], t_split[:, s, jt, :],
                                        start=first and s == 0, stop=True, skip_group_check=True)
                ins.then_inc(S["pe_group"], 1)

            pe.wait_ge(S["pre_ready"], T)
            n = 0
            for g in range(2):
                if g:
                    pe.wait_ge(S["w_ready"], HALF)
                for first, diagonal in pass_loops(g):
                    skip = 1 if diagonal else 0
                    if skip:
                        for u in range(AR):
                            s_step(first + u, n + u, u, u == 0)
                    with pe.Fori(skip, HALF // AR) as p:
                        for u in range(AR):
                            s_step(AR * p + (first + u), AR * p + (n + u), u, False)
                    n += HALF

            def y_tile(i, u, reused):
                if reused is not None:
                    pe.wait_ge(S["y_used"], reused)
                for j in range(T):
                    if type(i) is int and i == 0:
                        pe.wait_ge(S["w_ready"], j + 1)
                    for s in range(2):
                        ins = pe.matmul(psum[:, u, :], adjT[:, j, bass.ts(i, P)], w_split[:, s, j, :],
                                        start=j == 0 and s == 0, stop=j == T - 1 and s == 1)
                ins.then_inc(S["y_ready"], 1)

            pe.wait_ge(S["w_ready"], HALF + 2)
            y_tile(0, 0, None)
            y_tile(1, 1, None)
            with pe.Fori(1, T // 2) as p:
                for u in range(2):
                    y_tile(2 * p + u, u, 2 * p + u - 1)


_INS = ["x", "adj", "L0_gnn_W_seq", "L0_gnn_a1", "L0_gnn_a2", "L0_gnn_W_out", "L0_gnn_b_out"]


def kernel(**inputs):
    import numpy as _np
    import concourse.bacc as _bacc
    from concourse import mybir as _mybir
    from concourse.bass_utils import run_bass_kernel_spmd as _run

    nc = _bacc.Bacc("TRN2", target_bir_lowering=False, num_devices=1)
    arrays, args = {}, []
    for name in _INS:
        a = _np.ascontiguousarray(inputs[name])
        arrays[f"in_{name}_dram"] = a
        args.append(nc.dram_tensor(f"in_{name}_dram", a.shape, _mybir.dt.from_np(a.dtype), kind="ExternalInput").ap())
    args.append(nc.dram_tensor("out_0_dram", (N, D), F32, kind="ExternalOutput").ap())
    gat_gcn_kernel(nc, *args)
    r = _run(nc, [arrays], core_ids=[0])
    return r.results[0]["out_0_dram"]
```

```python
from contextlib import ExitStack

import concourse.bass as bass
from concourse import mybir

F32 = mybir.dt.float32
F16 = mybir.dt.float16
BF16 = mybir.dt.bfloat16
ALU = mybir.AluOpType
ACT = mybir.ActivationFunctionType
AX = mybir.AxisListType
RMAX = bass.bass_isa.ReduceOp.max

P = 128
N, D, H = 2048, 512, 16
DH = D // H
T = N // P
KC = D // P
ALPHA = 0.2
EPS = 1e-5
STEP = float(2 ** 30)
TOP = float(2 ** 14)
VC = DH + 1
PAIR = 2 * VC
SPLIT = 2 * PAIR
WH = D // 2 + H
GROUP = 2
NG = T // GROUP
SLOTS = 4
T_SCALE = 2.0 ** 8
W_SCALE = 2.0 ** 5
HALF = T // 2
AR = 4

VECTOR_STEPS = (1, 3, 5)
VALUES_AT, LOW_AT, FINISH_AT = 1, 5, (3, 4, 6, 7)
TAKE_AT, HIGH_AT = 1, 4


def bank_of(i):
    return (i // 3, i % 3 * SPLIT) if i < 12 else (4 + (i - 12) // 2, (i - 12) % 2 * SPLIT)


def first_in_bank(i):
    return bank_of(i)[1] == 0


def gat_gcn_kernel(nc, x_d, adj_d, wseq_d, a1_d, a2_d, wout_d, bout_d, out_d):
    ctx = ExitStack()
    with ctx:
        def sb(name, shape, dt):
            return ctx.enter_context(nc.sbuf_tensor(name, shape, dt))

        def sem(name):
            return ctx.enter_context(nc.semaphore(name))

        s1_d = nc.dram_tensor("s1_rows", [H, N], F32, kind="Internal").ap()

        adjT = sb("adjT", [P, T, N], F16)
        hid = sb("hid", [P, T * D], F32)
        seq = sb("seq", [P, T * D], F32)
        area1 = sb("area1", [P, 8192], F32)
        area2 = sb("area2", [P, 10432], F32)
        ident = sb("ident", [P, P], F32)
        ident16 = sb("ident16", [P, P], F16)
        bd = sb("bd", [P, H, T, 2], F32)
        rho = sb("rho", [P, H, T], F32)
        big_s2 = sb("big_s2", [P, H, T], F32)
        rowsum = sb("rowsum", [P, T], F32)
        degree = sb("degree", [P, T], F32)
        dinv = sb("dinv", [P, 3, T], F32)
        stat = sb("stat", [P, 2, H], F32)
        gstat = sb("gstat", [P, 2, H], F32)
        mv = sb("mv", [P, 2, 2], F32)
        rstd = sb("rstd", [P, 2], F32)
        shift = sb("shift", [P, 2], F32)
        power = sb("power", [P, T], F32)
        eps = sb("eps", [P, 1], F32)
        minus = sb("minus", [P, 1], F32)
        bst = sb("bst", [P, 2, 6], F32)
        rden = sb("rden", [P, T], F32)

        seq_t = seq[:, :].rearrange("p (t n) -> p t n", t=T)
        seq_h = seq[:, :].rearrange("p (t h d) -> p t h d", t=T, h=H)
        hid_h = hid[:, :].rearrange("p (t h d) -> p t h d", t=T, h=H)
        x_in = hid[:, 0:1024].rearrange("p (u n) -> p u n", u=2)
        xT = hid[:, 1024:2048].rearrange("p (u c n) -> p u c n", u=2, c=KC)
        w_all = hid[:, 2048:2048 + KC * 2 * WH].rearrange("p (c e n) -> p c e n", c=KC, e=2)
        s12 = hid[:, 4224:4736].rearrange("p (t e h) -> p t e h", t=T, e=2)
        vmax = hid[:, 4736:4992].rearrange("p (t h) -> p t h", t=T)
        vmin = hid[:, 4992:5248].rearrange("p (t h) -> p t h", t=T)
        q_row = hid[:, 5248:5504].rearrange("p (h t) -> p h t", h=H)
        q_hi = hid[:, 5504:5760].rearrange("p (h t) -> p h t", h=H)
        avec = hid[:, 5760:5824].rearrange("p (e d) -> p e d", e=2)
        col_acc = hid[:, 5824:6848].bitcast(F16).rearrange("p (j n) -> p j n", j=T)
        wtmp = [hid[:, 5824:7872], area1[:, 6144:8192]]
        a_in = area1[:, 0:4096].rearrange("p (u n) -> p u n", u=2)
        a16 = area1[:, 4096:6144].bitcast(F16).rearrange("p (u n) -> p u n", u=2)
        s1_now = hid[:, 7872:7904].rearrange("p (u h) -> p u h", u=2)
        s1row = area2[0:H, 8320:8320 + N]
        ring = area1[:, :].bitcast(F16).rearrange("p (s k n) -> p s k n", s=SLOTS, k=GROUP)
        ring_bf = area1[:, :].bitcast(BF16).rearrange("p (s k n) -> p s k n", s=SLOTS, k=GROUP)
        s1b = area2[:, 0:4096].rearrange("p (u n) -> p u n", u=2)
        rhs = area2[:, 4096:7264].bitcast(F16).rearrange("p (u t e c) -> p u t e c", u=2, t=T, e=3)
        val = area2[:, 7264:8320].rearrange("p (t e c) -> p t e c", t=T, e=2)
        sums = area2[:, 8320:10432].rearrange("p (t e c) -> p t e c", t=T, e=2)
        wout = seq[:, 0:2048].rearrange("p (c n) -> p c n", c=KC)
        x_res = seq[:, 2048:3072].rearrange("p (u n) -> p u n", u=2)
        bout = seq[:, 3072:3584]
        h_in = area2[:, 6144:7168].rearrange("p (u n) -> p u n", u=2)
        hT = area2[:, 7168:8192].rearrange("p (u c n) -> p u c n", u=2, c=KC)
        pre = area2[:, 8192:9216].rearrange("p (u n) -> p u n", u=2)
        expm = area2[:, 9216:10240].rearrange("p (u n) -> p u n", u=2)
        rows = area1[:, :].rearrange("p (t n) -> p t n", t=T)
        t_split = hid[:, :].bitcast(F16).rearrange("p (t s n) -> p s t n", s=2, t=T)
        w_split = seq[:, :].bitcast(F16).rearrange("p (s t n) -> p s t n", s=2, t=T)
        a_half = area2[:, 0:4096].rearrange("p (u n) -> p u n", u=AR)
        s_ring = area2[:, 4096:6144].bitcast(F16).rearrange("p (u n) -> p u n", u=AR)

        psum = ctx.enter_context(nc.psum_tensor("psum", [P, 8, 512], F32))
        psum16 = psum[:, :, :].bitcast(F16)

        names = """ident_ready a12_loaded wseq_loaded w_a2 wa_ready x_transposed xT_ready
            a_cast a_transposed adj_evac_v adj_evac_s seq_mm seq_evac s1_ready s2_stats stats_reduced tables_in
            tables_exp s1_transposed s1_copied s1_stored dinv_ready
            val_ready high_ready low_ready rhs_ready step_s mask_ready pe_group sums_ready bout_loaded wout_loaded
            hid_ready h_copied h_transposed hT_ready proj_done pre_ready exp_done row_ready var_ready rstd_ready
            t_high t_ready x_norm s_ready bank_done w_high w_ready y_ready y_used out_done stored
            v_chain p_chain""".split()
        S = {n: sem(n) for n in names}
        x_loaded = [sem(f"x_loaded{u}") for u in range(2)]
        a_loaded = [sem(f"a_loaded{u}") for u in range(2)]
        s1b_loaded = [sem(f"s1b_loaded{u}") for u in range(2)]
        xr_loaded = [sem(f"xr_loaded{u}") for u in range(2)]
        ah_loaded = [sem(f"ah_loaded{u}") for u in range(AR)]

        x_t = x_d.rearrange("(t p) n -> p t n", p=P)
        adj_t = adj_d.rearrange("(t p) n -> p t n", p=P)
        out_t = out_d.rearrange("(t p) n -> p t n", p=P)

        def w_head(e):
            return w_all[:, :, e, 0:D // 2].rearrange("p c (h d) -> p c h d", d=DH)

        def a_head(a):
            return avec[:, a:a + 1, :].unsqueeze(1).to_broadcast([P, KC, H // 2, DH])

        def fold_view(a, e):
            return wtmp[a].rearrange("p (e c h d) -> p e c h d", e=2, c=KC, d=DH)[:, e]

        block = ctx.enter_context(nc.Block())

        def u_count(h, u):
            return 8 * h + (16 - 8 * u)

        def pass_loops(g):
            return ((HALF * g, True), (HALF * (1 - g), False))

        @block.sync
        def _(sp):
            for c in range(KC):
                sp.dma_start(w_all[:, c, :, 0:D // 2], wseq_d[c * P:(c + 1) * P, :].rearrange("p (e n) -> p e n", e=2)
                             ).then_inc(S["wseq_loaded"], 16)
            for a, d in enumerate((a1_d, a2_d)):
                sp.dma_start(avec[:, a, :], d.rearrange("(o n) -> o n", o=1).to_broadcast([P, DH])
                             ).then_inc(S["a12_loaded"], 16)

            def load(t, u, again):
                if again is not None:
                    sp.wait_ge(S["x_transposed"], again)
                sp.dma_start(x_in[:, u, :], x_t[:, t, :]).then_inc(x_loaded[u], 16)
                if again is not None:
                    sp.wait_ge(S["a_cast"], again)
                sp.dma_start(a_in[:, u, :], adj_t[:, t, :]).then_inc(a_loaded[u], 16)

            for u in range(2):
                load(u, u, None)
            with sp.Fori(1, T // 2) as p:
                for u in range(2):
                    load(2 * p + u, u, 2 * p + u - 1)
            sp.wait_ge(S["s1_copied"], T)
            sp.dma_start(s1_d, s1row).then_inc(S["s1_stored"], 16)
            sp.wait_ge(S["s1_stored"], 16)

            def spread(h, u):
                sp.dma_start(s1b[:, u, :], s1_d[bass.ds(h, 1), :].to_broadcast([P, N])).then_inc(s1b_loaded[u], 16)

            spread(0, 0)
            spread(1, 1)
            with sp.Fori(1, H // 2) as p:
                for u in range(2):
                    sp.wait_ge(S["mask_ready"], NG * (2 * p + u - 1))
                    spread(2 * p + u, u)
            sp.wait_ge(S["rhs_ready"], H)
            sp.dma_start(wout, wout_d.rearrange("(c p) n -> p c n", p=P)).then_inc(S["wout_loaded"], 16)
            sp.dma_start(bout, bout_d.rearrange("(o n) -> o n", o=1).to_broadcast([P, D])
                         ).then_inc(S["bout_loaded"], 16)
            for u in range(2):
                sp.dma_start(x_res[:, u, :], x_t[:, u, :]).then_inc(xr_loaded[u], 16)
            sp.wait_ge(S["mask_ready"], NG * H)
            for u in range(AR):
                sp.dma_start(a_half[:, u, :], adj_t[:, u, 0:1024]).then_inc(ah_loaded[u], 16)
            with sp.Fori(1, T // 2) as p:
                for u in range(2):
                    sp.wait_ge(S["row_ready"], 2 * p + u - 1)
                    sp.dma_start(x_res[:, u, :], x_t[:, 2 * p + u, :]).then_inc(xr_loaded[u], 16)
            done = AR
            for g in range(2):
                for first, _ in pass_loops(g):
                    skip = 1 if done == AR and g == 0 and first == 0 else 0
                    with sp.Fori(skip, HALF // AR) as p:
                        for u in range(AR):
                            sp.wait_ge(S["s_ready"], AR * p + u + 1 + (done - AR) - AR * skip)
                            sp.dma_start(a_half[:, u, :],
                                         adj_t[:, AR * p + (first + u), 1024 * g:1024 * g + 1024]
                                         ).then_inc(ah_loaded[u], 16)
                    done += HALF - AR * skip
            with sp.Fori(0, T) as t:
                sp.wait_ge(S["out_done"], t + 1)
                sp.dma_start(out_t[:, t, :], rows[:, t, :]).then_inc(S["stored"], 16)
            sp.wait_ge(S["stored"], 16 * T)

        @block.gpsimd
        def _(pool):
            pool.memset(ident[:, :], 0.0).then_inc(S["ident_ready"], 1)
            pool.wait_ge(S["ident_ready"], 1)
            pool.affine_select(out=ident[:, :], in_=ident[:, :], compare_op=ALU.not_equal, fill=1.0,
                               base=0, pattern=[[-1, P]], channel_multiplier=1).then_inc(S["ident_ready"], 1)
            pool.wait_ge(S["ident_ready"], 2)
            pool.tensor_copy(ident16[:, :], ident[:, :]).then_inc(S["ident_ready"], 1)
            pool.wait_ge(S["wseq_loaded"], 16 * KC)
            pool.wait_ge(S["a12_loaded"], 32)
            for e in range(2):
                ins = pool.tensor_tensor(fold_view(1, e), w_head(e), a_head(1), ALU.mult)
            ins.then_inc(S["w_a2"], 1)
            pool.memset(eps[:, :], EPS)
            pool.memset(minus[:, :], -1.0)
            pool.memset(power[:, :], -0.5).then_inc(S["p_chain"], 1)
            pool.wait_ge(S["wa_ready"], 1)
            pool.memset(col_acc, 0.0).then_inc(S["p_chain"], 1)
            with pool.Fori(0, T) as t:
                pool.wait_ge(S["adj_evac_v"], t + 1)
                pool.wait_ge(S["adj_evac_s"], t + 1)
                pool.wait_ge(S["p_chain"], t + 2)
                pool.tensor_tensor(col_acc, col_acc, adjT[:, :, bass.ts(t, P)], ALU.add
                                   ).then_inc(S["p_chain"], 1)
            pool.wait_ge(S["s2_stats"], 1)
            pool.partition_all_reduce(gstat[:, :, :].rearrange("p a h -> p (a h)"),
                                      stat[:, :, :].rearrange("p a h -> p (a h)"), P, RMAX
                                      ).then_inc(S["stats_reduced"], 1)

            links = [2 + T]

            def link(ins):
                links[0] += 1
                ins.then_inc(S["p_chain"], 1)
                pool.wait_ge(S["p_chain"], links[0])

            pool.wait_ge(S["p_chain"], links[0])
            pool.wait_ge(S["a_cast"], T)
            width = P // 2
            while width:
                link(pool.tensor_tensor(col_acc[:, :, 0:width], col_acc[:, :, 0:width],
                                        col_acc[:, :, width:2 * width], ALU.add))
                width //= 2
            link(pool.tensor_copy(degree[:, :], col_acc[:, :, 0]))
            link(pool.tensor_tensor(degree[:, :], degree[:, :], rowsum[:, :], ALU.add))
            link(pool.tensor_scalar(degree[:, :], degree[:, :], 0.5, 1.0, ALU.mult, ALU.add))
            link(pool.tensor_scalar(dinv[:, 1, :], degree[:, :], 0.0, None, ALU.is_gt))
            link(pool.tensor_scalar(degree[:, :], degree[:, :], 1e-30, None, ALU.max))
            link(pool.tensor_tensor(dinv[:, 0, :], degree[:, :], power[:, :], ALU.pow))
            link(pool.tensor_tensor(dinv[:, 0, :], dinv[:, 0, :], dinv[:, 1, :], ALU.mult))
            link(pool.tensor_scalar(dinv[:, 1, :], dinv[:, 0, :], T_SCALE, None, ALU.mult))
            pool.tensor_scalar(dinv[:, 2, :], dinv[:, 0, :], 0.5 * W_SCALE / T_SCALE, None, ALU.mult
                               ).then_inc(S["dinv_ready"], 1)

            def norm_factors(t, u, used=None):
                pool.wait_ge(S["var_ready"], t + 1)
                pool.tensor_tensor(mv[:, u, 1:2], mv[:, u, 1:2], eps[:, :], ALU.add).then_inc(S["p_chain"], 1)
                if used is not None:
                    pool.wait_ge(S["x_norm"], used)
                pool.wait_ge(S["p_chain"], 3 * t + (links[0] + 1))
                pool.tensor_tensor(rstd[:, u:u + 1], mv[:, u, 1:2], power[:, 0:1], ALU.pow
                                   ).then_inc(S["p_chain"], 1)
                pool.wait_ge(S["p_chain"], 3 * t + (links[0] + 2))
                pool.tensor_tensor(shift[:, u:u + 1], mv[:, u, 0:1], rstd[:, u:u + 1], ALU.mult
                                   ).then_inc(S["p_chain"], 1)
                pool.wait_ge(S["p_chain"], 3 * t + (links[0] + 3))
                pool.tensor_tensor(shift[:, u:u + 1], shift[:, u:u + 1], minus[:, :], ALU.mult
                                   ).then_inc(S["rstd_ready"], 1)

            norm_factors(0, 0)
            norm_factors(1, 1)
            with pool.Fori(1, T // 2) as p:
                for u in range(2):
                    norm_factors(2 * p + u, u, 2 * p + u - 1)
            with pool.Fori(T // 2, T) as p:
                for u in range(2):
                    norm_factors(2 * p + u, u)

        @block.scalar
        def _(act):
            def cast(t, u, reused, count):
                act.wait_ge(a_loaded[u], 16 * count)
                if reused is not None:
                    act.wait_ge(S["a_transposed"], reused)
                act.activation(a16[:, u, :], a_in[:, u, :], ACT.Copy,
                               accum_out=rowsum[:, bass.ds(t, 1)]).then_inc(S["a_cast"], 1)

            def s1_part(t, u):
                act.wait_ge(S["s1_transposed"], t + 1)
                act.activation(s1row[:, bass.ts(t, P)], psum[0:H, 6 + u, 0:P], ACT.Copy, scale=-STEP
                               ).then_inc(S["s1_copied"], 1)

            def evacuate_x(t, u):
                act.wait_ge(S["x_transposed"], t + 1)
                act.activation(xT[:, u, :, :].rearrange("p c n -> p (c n)"), psum[:, 6 + u, :], ACT.Copy
                               ).then_inc(S["xT_ready"], 1)

            def evacuate_adj(t, u):
                act.wait_ge(S["a_transposed"], 2 * t + 2)
                act.activation(adjT[:, 8:16, bass.ts(t, P)],
                               psum16[:, 5, :].rearrange("p (j n) -> p j n", j=8), ACT.Copy
                               ).then_inc(S["adj_evac_s"], 1)
                if type(t) is not int or t:
                    s1_part(t - 1, 1 - u)

            def evacuate(t, u):
                evacuate_x(t, u)
                evacuate_adj(t, u)

            evacuate_x(0, 0)
            cast(0, 0, None, 1)
            cast(1, 1, None, 1)
            evacuate_adj(0, 0)
            with act.Fori(0, T // 2 - 1) as p:
                evacuate(2 * p + 1, 1)
                cast(2 * p + 2, 0, 4 * p + 2, p + 2)
                evacuate(2 * p + 2, 0)
                cast(2 * p + 3, 1, 4 * p + 4, p + 2)
            evacuate(T - 1, 1)
            s1_part(T - 1, 1)

            act.wait_ge(S["tables_in"], 1)
            act.activation(bd[:, :, :, 0], q_row, ACT.Exp).then_inc(S["tables_exp"], 1)
            act.activation(bd[:, :, :, 1], q_row, ACT.Exp, scale=ALPHA).then_inc(S["tables_exp"], 1)
            act.activation(rho[:, :, :], q_hi, ACT.Exp, scale=ALPHA - 1.0).then_inc(S["tables_exp"], 1)

            def high(h, u):
                act.wait_ge(S["val_ready"], h + 1)
                if type(h) is not int or h >= 2:
                    act.wait_ge(S["pe_group"], NG * (h - 1))
                act.activation(rhs[:, u, :, 0:3:2, 0:VC], val, ACT.Copy).then_inc(S["high_ready"], 1)

            def steps(h, u, g, fresh=False):
                q = NG * h + g
                if not fresh:
                    act.wait_ge(S["pe_group"], q - SLOTS + 1)
                if g == 0:
                    act.wait_ge(s1b_loaded[u], u_count(h, u))
                for k in range(1 if g in VECTOR_STEPS else 2):
                    j = GROUP * g + k
                    ins = act.activation(ring_bf[:, g % SLOTS, k, :], s1b[:, u, :], ACT.Relu,
                                         bias=big_s2[:, h, j:j + 1], scale=-1.0)
                ins.then_inc(S["step_s"], 1)

            def take_banks(lo, hi):
                k = 3 if hi <= 4 else 2
                act.activation(sums[:, 3 * lo:3 * lo + k * (hi - lo), :, :].rearrange(
                                   "p (b k) e c -> p b (k e c)", b=hi - lo),
                               psum[:, lo:hi, 0:k * SPLIT], ACT.Copy).then_inc(S["sums_ready"], 1)

            def take_sums(h, first=4):
                act.wait_ge(S["pe_group"], NG * (h + 1))
                act.wait_ge(S["hid_ready"], h + 1)
                take_banks(0, first)
                if first < 4:
                    take_banks(first, 4)
                take_banks(4, 6)

            high(0, 0)
            act.wait_ge(S["a_transposed"], 2 * T)
            for g in range(NG):
                steps(0, 0, g, fresh=g < SLOTS)
                if g == HIGH_AT:
                    high(1, 1)
            with act.Fori(0, H // 2 - 1) as p:
                for h, u in ((2 * p + 1, 1), (2 * p + 2, 0)):
                    for g in range(NG):
                        steps(h, u, g)
                        if g == TAKE_AT:
                            take_sums(h - 1)
                        if g == HIGH_AT:
                            high(h + 1, 1 - u)
            for g in range(NG):
                steps(H - 1, 1, g)
                if g == TAKE_AT:
                    take_sums(H - 2)
            take_sums(H - 1, first=1)

            def copy_h(t, u):
                if type(t) is not int or t >= 2:
                    act.wait_ge(S["h_transposed"], t - 1)
                act.activation(h_in[:, u, :], hid[:, bass.ts(t, D)], ACT.Copy).then_inc(S["h_copied"], 1)

            def copy_hT(t, u):
                act.wait_ge(S["h_transposed"], t + 1)
                if type(t) is not int or t >= 2:
                    act.wait_ge(S["proj_done"], t - 1)
                act.activation(hT[:, u, :, :].rearrange("p c n -> p (c n)"), psum[:, 6 + u, :], ACT.Copy
                               ).then_inc(S["hT_ready"], 1)

            def exp_t(t, u):
                act.wait_ge(S["pre_ready"], t + 1)
                act.activation(expm[:, u, :], expm[:, u, :], ACT.Exp).then_inc(S["exp_done"], 1)

            def norm_high(t, u):
                act.wait_ge(S["rstd_ready"], t + 1)
                act.activation(rows[:, t, :], rows[:, t, :], ACT.Identity, scale=rstd[:, u:u + 1],
                               bias=shift[:, u:u + 1]).then_inc(S["x_norm"], 1)
                act.wait_ge(S["x_norm"], t + 1)
                act.activation(t_split[:, 0, t, :], rows[:, t, :], ACT.Copy,
                               scale=dinv[:, 1, bass.ds(t, 1)]).then_inc(S["t_high"], 1)

            act.wait_ge(S["dinv_ready"], 1)
            act.wait_ge(S["hid_ready"], H + 1)
            copy_h(0, 0)
            copy_h(1, 1)
            copy_hT(0, 0)
            copy_h(2, 0)
            copy_hT(1, 1)
            act.wait_ge(S["hid_ready"], H + 2)
            copy_h(3, 1)
            for t in range(2):
                exp_t(t, t)
                copy_hT(t + 2, t)
                copy_h(t + 4, t)
            with act.Fori(1, T // 2 - 2) as p:
                for u in range(2):
                    t = 2 * p + u
                    exp_t(t, u)
                    copy_hT(t + 2, u)
                    copy_h(t + 4, u)
                    norm_high(t - 2, u)
            for t in range(T - 4, T):
                exp_t(t, t % 2)
                if t < T - 2:
                    copy_hT(t + 2, t % 2)
                norm_high(t - 2, t % 2)
            for t in range(T - 2, T):
                norm_high(t, t % 2)
            for i in range(T):
                act.wait_ge(S["bank_done"], i + 1)
                act.activation(w_split[:, 0, i, :], psum[:, i % HALF, :], ACT.Copy,
                               scale=dinv[:, 2, i:i + 1]).then_inc(S["w_high"], 1)

        @block.vector
        def _(dve):
            links = [0]

            def link(ins, base=0):
                links[0] += 1
                ins.then_inc(S["v_chain"], 1)
                dve.wait_ge(S["v_chain"], base + links[0])

            dve.wait_ge(S["wseq_loaded"], 16 * KC)
            dve.wait_ge(S["a12_loaded"], 32)
            dve.tensor_tensor(fold_view(0, 0), w_head(0), a_head(0), ALU.mult)
            link(dve.tensor_tensor(fold_view(0, 1), w_head(1), a_head(0), ALU.mult))
            for a in range(2):
                if a:
                    dve.wait_ge(S["w_a2"], 1)
                for e in range(2):
                    ins = dve.reduce_sum(w_all[:, :, a, D // 2 + e * H // 2:D // 2 + (e + 1) * H // 2],
                                         fold_view(a, e), axis=AX.X)
            ins.then_inc(S["wa_ready"], 1)

            def first_layer(t, u):
                dve.wait_ge(S["a_transposed"], 2 * t + 1)
                dve.tensor_copy(adjT[:, 0:8, bass.ts(t, P)],
                                psum16[:, 4, :].rearrange("p (j n) -> p j n", j=8)).then_inc(S["adj_evac_v"], 1)
                dve.wait_ge(S["seq_mm"], t + 1)
                banks = psum[:, 2 * u:2 * u + 2, :]
                if type(t) is not int or t >= 2:
                    dve.wait_ge(S["s1_transposed"], t - 1)
                dve.tensor_copy(s1_now[:, u, :], banks[:, 0, D // 2:WH]).then_inc(S["s1_ready"], 1)
                dve.tensor_copy(s12[:, t, :, :], banks[:, :, D // 2:WH])
                for extreme, op in ((vmax, ALU.max), (vmin, ALU.min)):
                    dve.tensor_reduce(extreme[:, t, :].rearrange("p (e h) -> p e h", e=2),
                                      banks[:, :, 0:D // 2].rearrange("p e (h d) -> p e h d", d=DH),
                                      axis=AX.X, op=op)
                dve.tensor_copy(seq_t[:, t, :].rearrange("p (e n) -> p e n", e=2), banks[:, :, 0:D // 2]
                                ).then_inc(S["seq_evac"], 1)

            for t in range(2):
                first_layer(t, t)
            with dve.Fori(1, T // 2) as p:
                for u in range(2):
                    first_layer(2 * p + u, u)

            dve.wait_ge(S["seq_evac"], T)
            s1 = s12[:, :, 0, :].rearrange("p t h -> p h t")
            s2 = s12[:, :, 1, :].rearrange("p t h -> p h t")
            dve.reduce_max(stat[:, 0, :], s2, axis=AX.X)
            dve.reduce_max(stat[:, 1, :], vmax.rearrange("p t h -> p h t"), axis=AX.X)
            link(dve.tensor_reduce(gstat[:, 0, :], vmin.rearrange("p t h -> p h t"), axis=AX.X, op=ALU.min))
            dve.scalar_tensor_tensor(stat[:, 1, :], gstat[:, 0, :], -1.0, stat[:, 1, :], ALU.mult, ALU.max
                                     ).then_inc(S["s2_stats"], 1)
            dve.tensor_scalar(big_s2[:, :, :], s2, STEP, None, ALU.mult).then_inc(S["hid_ready"], 1)
            dve.wait_ge(S["stats_reduced"], 1)
            m2 = gstat[:, 0, :].unsqueeze(2).to_broadcast([P, H, T])
            dve.tensor_tensor(q_row, s2, m2, ALU.subtract)
            link(dve.tensor_tensor(q_hi, s1, m2, ALU.add))
            link(dve.tensor_scalar(gstat[:, 1, :], gstat[:, 1, :], 1.0, None, ALU.max))
            dve.tensor_scalar(q_hi, q_hi, 0.0, None, ALU.max).then_inc(S["tables_in"], 1)
            link(dve.reciprocal(gstat[:, 1, :], gstat[:, 1, :]))
            link(dve.tensor_scalar(gstat[:, 1, :], gstat[:, 1, :], TOP, None, ALU.mult))
            dve.wait_ge(S["tables_exp"], 2)
            link(dve.tensor_tensor(bd[:, :, :, :].rearrange("p h t e -> p h (t e)"),
                                   bd[:, :, :, :].rearrange("p h t e -> p h (t e)"),
                                   gstat[:, 1, :].unsqueeze(2).to_broadcast([P, H, 2 * T]), ALU.mult))
            n0 = links[0]

            def values(h):
                dve.tensor_copy(val[:, :, :, DH], bd[:, h, :, :])
                dve.tensor_tensor(val[:, :, :, 0:DH], seq_h[:, :, h, :].unsqueeze(2).to_broadcast([P, T, 2, DH]),
                                  bd[:, h, :, :].unsqueeze(3).to_broadcast([P, T, 2, DH]), ALU.mult
                                  ).then_inc(S["val_ready"], 1)

            def low(h, u):
                dve.wait_ge(S["val_ready"], h + 1)
                dve.wait_ge(S["high_ready"], h + 1)
                dve.tensor_tensor(rhs[:, u, :, 0:3:2, VC:PAIR], val, rhs[:, u, :, 0:3:2, 0:VC], ALU.subtract
                                  ).then_inc(S["low_ready"], 1)
                dve.wait_ge(S["low_ready"], h + 1)
                dve.tensor_scalar(rhs[:, u, :, 1, :], rhs[:, u, :, 2, :], -1.0, None, ALU.mult
                                  ).then_inc(S["rhs_ready"], 1)

            def masks(h, u, g, fresh=False):
                q = NG * h + g
                k = 2
                if g in VECTOR_STEPS:
                    k = 1
                    j = GROUP * g + 1
                    if not fresh:
                        dve.wait_ge(S["pe_group"], q - SLOTS + 1)
                    dve.wait_ge(s1b_loaded[u], u_count(h, u))
                    dve.scalar_tensor_tensor(ring[:, g % SLOTS, 1, :], s1b[:, u, :], big_s2[:, h, j:j + 1],
                                             adjT[:, j, :], ALU.is_lt, ALU.mult)
                j = GROUP * g
                dve.wait_ge(S["step_s"], q + 1)
                dve.tensor_tensor(ring[:, g % SLOTS, 0:k, :], ring_bf[:, g % SLOTS, 0:k, :], adjT[:, j:j + k, :],
                                  ALU.min).then_inc(S["mask_ready"], 1)

            V = S["v_chain"]

            def finish(h, part, base, tiles=slice(0, T), taken=2):
                n = tiles.stop - tiles.start
                side = [sums[:, tiles, e, 0:VC] for e in range(2)]
                if part == 0:
                    dve.wait_ge(S["sums_ready"], 2 * h + taken)
                    dve.tensor_tensor(sums[:, tiles, :, 0:VC], sums[:, tiles, :, 0:VC], sums[:, tiles, :, VC:PAIR],
                                      ALU.add).then_inc(V, 1)
                elif part == 1:
                    dve.wait_ge(V, base + 1)
                    dve.tensor_tensor(side[1], side[1], rho[:, h, tiles].unsqueeze(2).to_broadcast([P, n, VC]),
                                      ALU.mult).then_inc(V, 1)
                elif part == 2:
                    dve.wait_ge(V, base + 2)
                    dve.tensor_tensor(side[0], side[0], side[1], ALU.add).then_inc(V, 1)
                else:
                    dve.wait_ge(V, base + 3)
                    dve.reciprocal(rden[:, tiles], sums[:, tiles, 0, DH]).then_inc(V, 1)
                    dve.wait_ge(V, base + 4)
                    dve.tensor_tensor(hid_h[:, tiles, h, :], sums[:, tiles, 0, 0:DH],
                                      rden[:, tiles].unsqueeze(2).to_broadcast([P, n, DH]), ALU.mult
                                      ).then_inc(S["hid_ready"], 1)

            def between(h, u, g, last=False):
                if g == VALUES_AT and not last:
                    values(h + 1)
                if g == LOW_AT and not last:
                    low(h + 1, 1 - u)
                if g in FINISH_AT and not (type(h) is int and h == 0):
                    finish(h - 1, FINISH_AT.index(g), n0 + 4 * (h - 1))

            dve.wait_ge(S["tables_exp"], 3)
            values(0)
            low(0, 0)
            for g in range(NG):
                masks(0, 0, g, fresh=g < SLOTS)
                between(0, 0, g)
            dve.wait_ge(S["dinv_ready"], 1)
            with dve.Fori(0, H // 2 - 1) as p:
                for h, u in ((2 * p + 1, 1), (2 * p + 2, 0)):
                    for g in range(NG):
                        masks(h, u, g)
                        between(h, u, g)
            for g in range(NG):
                masks(H - 1, 1, g)
                between(H - 1, 1, g, last=True)
            for tiles, taken, base in ((slice(0, 3), 1, n0 + 4 * (H - 1)), (slice(3, T), 3, n0 + 4 * H)):
                for part in range(4):
                    finish(H - 1, part, base, tiles, taken)
            base = n0 + 4 * (H + 1)

            def s_tile(g, jt, n, u, diagonal, used, link_at=None):
                dve.wait_ge(ah_loaded[u], 4 * (n - u) + 16)
                if used is not None:
                    dve.wait_ge(*used)
                ins = dve.tensor_tensor(s_ring[:, u, :], a_half[:, u, :],
                                        adjT[:, jt, 1024 * g:1024 * g + 1024], ALU.add)
                if diagonal:
                    ins.then_inc(V, 1)
                    dve.wait_ge(V, link_at)
                    spot = s_ring[:, u, bass.ds((jt - HALF * g) * P, P)]
                    ins = dve.scalar_tensor_tensor(spot, ident[:, :], 2.0, spot, ALU.mult, ALU.add)
                ins.then_inc(S["s_ready"], 1)

            for u in range(2):
                s_tile(0, u, u, u, True, None, base + u + 1)
            base += 2

            def elu(t, u, count, base):
                later = type(t) is not int
                dve.wait_ge(S["proj_done"], t + 1)
                if later or t >= 1:
                    dve.wait_ge(S["row_ready"], t)
                if later or t >= 2:
                    dve.wait_ge(V, base)
                if later or t >= 4:
                    dve.wait_ge(S["rstd_ready"], t - 3)
                dve.tensor_tensor(pre[:, u, :], psum[:, u, :], bout, ALU.add).then_inc(V, 1)
                if later or t >= 2:
                    dve.bn_aggr(mv[:, u, :], bst[:, u, :]).then_inc(S["var_ready"], 1)
                dve.wait_ge(V, base + 1)
                dve.tensor_scalar(expm[:, u, :], pre[:, u, :], 0.0, None, ALU.min).then_inc(S["pre_ready"], 1)
                if later or t >= 3:
                    t_low(t - 3)
                dve.wait_ge(S["exp_done"], t + 1)
                dve.scalar_tensor_tensor(pre[:, u, :], pre[:, u, :], 0.0, expm[:, u, :], ALU.max, ALU.add
                                         ).then_inc(V, 1)
                if later or t >= 1:
                    dve.bn_stats(bst[:, 1 - u, :], rows[:, t - 1, :]).then_inc(V, 1)
                dve.wait_ge(V, base + 2)
                dve.wait_ge(xr_loaded[u], count)
                dve.scalar_tensor_tensor(rows[:, t, :], pre[:, u, :], -1.0, x_res[:, u, :], ALU.add, ALU.add
                                         ).then_inc(S["row_ready"], 1)

            def t_low(t):
                dve.wait_ge(S["x_norm"], t + 1)
                dve.wait_ge(S["t_high"], t + 1)
                dve.scalar_tensor_tensor(t_split[:, 1, t, :], rows[:, t, :], dinv[:, 1, bass.ds(t, 1)],
                                         t_split[:, 0, t, :], ALU.mult, ALU.subtract).then_inc(S["t_ready"], 1)

            dve.wait_ge(S["bout_loaded"], 16)
            for t in range(4):
                elu(t, t % 2, 16 * (t // 2 + 1), base + max(3 * t - 1, 0))
            with dve.Fori(2, T // 2) as p:
                for u in range(2):
                    elu(2 * p + u, u, 16 * p + 16, 6 * p + (base + 3 * u - 1))
            dve.wait_ge(V, base + 3 * T - 1)
            dve.wait_ge(S["rstd_ready"], T - 3)
            s_tile(0, 2, 2, 2, True, None, base + 3 * T)
            dve.bn_aggr(mv[:, 0, :], bst[:, 0, :]).then_inc(S["var_ready"], 1)
            s_tile(0, 3, 3, 3, True, None, base + 3 * T + 1)
            dve.wait_ge(S["row_ready"], T)
            dve.bn_stats(bst[:, 1, :], rows[:, T - 1, :]).then_inc(V, 1)
            links[0] = base + 3 * T + 2
            dve.wait_ge(V, links[0])
            dve.wait_ge(S["rstd_ready"], T - 2)
            dve.bn_aggr(mv[:, 1, :], bst[:, 1, :]).then_inc(S["var_ready"], 1)
            for t in range(T - 3, T):
                t_low(t)

            PG = NG * H
            with dve.Fori(1, HALF // AR) as p:
                for u in range(AR):
                    n = AR * p + u
                    s_tile(0, n, n, u, True, (S["pe_group"], n + (PG - AR + 1)), n + (links[0] - AR + 1))
            links[0] += HALF - AR
            with dve.Fori(HALF // AR, T // AR) as p:
                for u in range(AR):
                    n = AR * p + u
                    s_tile(0, n, n, u, False, (S["pe_group"], n + (PG - AR + 1)))
            for u in range(2):
                s_tile(1, HALF + u, T + u, u, True, (S["pe_group"], PG + T - AR + 1 + u), links[0] + u + 1)

            def w_low(i):
                dve.wait_ge(S["w_high"], i + 1)
                dve.scalar_tensor_tensor(w_split[:, 1, i, :], psum[:, i % HALF, :], dinv[:, 2, i:i + 1],
                                         w_split[:, 0, i, :], ALU.mult, ALU.subtract
                                         ).then_inc(S["w_ready"], 1)

            for i in range(HALF):
                w_low(i)
            for u in range(2, AR):
                s_tile(1, HALF + u, T + u, u, True, (S["bank_done"], HALF), links[0] + u + 1)
            links[0] += AR
            with dve.Fori(1, HALF // AR) as p:
                for u in range(AR):
                    n = AR * p + u
                    s_tile(1, n + HALF, n + T, u, True, (S["pe_group"], n + (PG + T - AR - 1)),
                           n + (links[0] - AR + 1))
            links[0] += HALF - AR
            with dve.Fori(HALF // AR, T // AR) as p:
                for u in range(AR):
                    n = AR * p + u
                    s_tile(1, n - HALF, n + T, u, False, (S["pe_group"], n + (PG + T - AR - 1)))
            for i in range(HALF, T):
                w_low(i)
            base = links[0]

            def last_norm(t, u):
                dve.wait_ge(S["rstd_ready"], t + (T + 1))
                dve.tensor_scalar(rows[:, t, :], pre[:, u, :], mv[:, u, 0:1], rstd[:, u:u + 1],
                                  ALU.subtract, ALU.mult).then_inc(S["out_done"], 1)

            def last_rows(t, u, first=False, reused=True):
                dve.wait_ge(S["y_ready"], t + 1)
                if reused:
                    dve.wait_ge(S["out_done"], t - 1)
                dve.scalar_tensor_tensor(pre[:, u, :], psum[:, u, :], 1.0 / W_SCALE, rows[:, t, :],
                                         ALU.mult, ALU.add).then_inc(S["y_used"], 1)
                dve.wait_ge(S["y_used"], t + 1)
                dve.bn_stats(bst[:, u, :], pre[:, u, :]).then_inc(V, 1)
                dve.wait_ge(V, base + 1 + t)
                if not first:
                    last_norm(t - 1, 1 - u)
                dve.bn_aggr(mv[:, u, :], bst[:, u, :]).then_inc(S["var_ready"], 1)

            last_rows(0, 0, first=True, reused=False)
            last_rows(1, 1, reused=False)
            last_rows(2, 0)
            with dve.Fori(1, T // 2 - 1) as p:
                last_rows(2 * p + 1, 1)
                last_rows(2 * p + 2, 0)
            last_rows(T - 1, 1)
            last_norm(T - 1, 1)

        @block.tensor
        def _(pe):
            pe.wait_ge(S["ident_ready"], 3)

            def turn_adj(t, u, reused):
                pe.wait_ge(S["a_cast"], t + 1)
                for half in range(2):
                    if reused:
                        pe.wait_ge(S["adj_evac_s" if half else "adj_evac_v"], t)
                    for b in range(8):
                        ins = pe.transpose(psum16[:, 4 + half, b * P:(b + 1) * P],
                                           a16[:, u, (8 * half + b) * P:(8 * half + b + 1) * P], ident16[:, :])
                    ins.then_inc(S["a_transposed"], 1)

            def turn_s1(t, u):
                pe.wait_ge(S["s1_ready"], t + 1)
                pe.transpose(psum[0:H, 6 + u, 0:P], s1_now[:, u, :], ident[:, :]).then_inc(S["s1_transposed"], 1)

            def project(t, u, count, later=True):
                pe.wait_ge(x_loaded[u], count)
                if later:
                    pe.wait_ge(S["s1_copied"], t - 1)
                for c in range(KC):
                    ins = pe.transpose(psum[:, 6 + u, c * P:(c + 1) * P], x_in[:, u, c * P:(c + 1) * P], ident[:, :])
                ins.then_inc(S["x_transposed"], 1)
                first = type(t) is int and t == 0
                if not first:
                    turn_adj(t, u, True)
                    turn_s1(t - 1, 1 - u)
                pe.wait_ge(S["xT_ready"], t + 1)
                if later:
                    pe.wait_ge(S["seq_evac"], t - 1)
                for lo, hi in ((0, D // 2), (D // 2, WH)) if first else ((0, WH),):
                    if first and lo:
                        pe.wait_ge(S["wa_ready"], 1)
                    for e in range(2):
                        for c in range(KC):
                            ins = pe.matmul(psum[:, 2 * u + e, lo:hi], xT[:, u, c, :], w_all[:, c, e, lo:hi],
                                            start=c == 0 and lo == 0, stop=c == KC - 1, skip_group_check=True)
                ins.then_inc(S["seq_mm"], 1)
                if first:
                    turn_adj(t, u, False)

            project(0, 0, 16, later=False)
            project(1, 1, 16, later=False)
            with pe.Fori(1, T // 2) as p:
                for u in range(2):
                    project(2 * p + u, u, 16 * p + 16)
            turn_s1(T - 1, 1)
            pe.wait_ge(S["seq_evac"], T)
            pe.wait_ge(S["adj_evac_v"], T)
            pe.wait_ge(S["adj_evac_s"], T)

            def head_group(h, u, g, reused):
                for k in range(GROUP):
                    j = GROUP * g + k
                    for i in range(T):
                        bank, col = bank_of(i)
                        if g == 0 and k == 0 and i in (0, 12) and reused is not None:
                            pe.wait_ge(S["sums_ready"], reused + (i == 12))
                        pe.matmul(psum[:, bank, col + PAIR:col + SPLIT], adjT[:, j, i * P:(i + 1) * P],
                                  rhs[:, u, j, 2, :], start=g == 0 and k == 0 and first_in_bank(i),
                                  stop=True, skip_group_check=True)
                pe.wait_ge(S["mask_ready"], NG * h + g + 1)
                for k in range(GROUP):
                    j = GROUP * g + k
                    for i in range(T):
                        bank, col = bank_of(i)
                        ins = pe.matmul(psum[:, bank, col:col + SPLIT], ring[:, g % SLOTS, k, i * P:(i + 1) * P],
                                        rhs[:, u, j, 0:2, :].rearrange("p e c -> p (e c)"), start=False,
                                        stop=True, skip_group_check=True)
                ins.then_inc(S["pe_group"], 1)

            def head(h, u, reused):
                pe.wait_ge(S["rhs_ready"], h + 1)
                for g in range(NG):
                    head_group(h, u, g, reused)

            pe.wait_ge(S["s1_copied"], T)
            head(0, 0, None)
            with pe.Fori(0, H // 2 - 1) as p:
                head(2 * p + 1, 1, 4 * p + 1)
                head(2 * p + 2, 0, 4 * p + 3)
            head(H - 1, 1, 2 * (H - 1) - 1)

            def turn_h(t, u, reused):
                pe.wait_ge(S["h_copied"], t + 1)
                if reused is not None:
                    pe.wait_ge(S["hT_ready"], reused)
                for c in range(KC):
                    ins = pe.transpose(psum[:, 6 + u, c * P:(c + 1) * P], h_in[:, u, c * P:(c + 1) * P], ident[:, :])
                ins.then_inc(S["h_transposed"], 1)

            def project_h(t, u, reused):
                pe.wait_ge(S["hT_ready"], t + 1)
                if reused is not None:
                    pe.wait_ge(S["pre_ready"], reused)
                for c in range(KC):
                    ins = pe.matmul(psum[:, u, :], hT[:, u, c, :], wout[:, c, :], start=c == 0, stop=c == KC - 1)
                ins.then_inc(S["proj_done"], 1)

            pe.wait_ge(S["wout_loaded"], 16)
            turn_h(0, 0, None)
            turn_h(1, 1, None)
            pe.wait_ge(S["sums_ready"], 2 * H + 1)
            project_h(0, 0, None)
            turn_h(2, 0, 1)
            project_h(1, 1, None)
            with pe.Fori(1, T // 2 - 1) as p:
                turn_h(2 * p + 1, 1, 2 * p)
                project_h(2 * p, 0, 2 * p - 1)
                turn_h(2 * p + 2, 0, 2 * p + 1)
                project_h(2 * p + 1, 1, 2 * p)
            turn_h(T - 1, 1, T - 2)
            project_h(T - 2, 0, T - 3)
            project_h(T - 1, 1, T - 2)

            def bank_step(b, jt, u, start):
                for s in range(2):
                    ins = pe.matmul(psum[:, b, :], s_ring[:, u, b * P:(b + 1) * P], t_split[:, s, jt, :],
                                    start=start and s == 0, stop=True, skip_group_check=True)
                return ins

            def s_step(jt, n, u, start=False, g=0):
                pe.wait_ge(S["t_ready"], jt + 1)
                pe.wait_ge(S["s_ready"], n + 1)
                for b in (2, 3, 4, 5, 6, 7, 0, 1) if start and g == 0 else range(HALF):
                    if start and g == 0 and b == 0:
                        pe.wait_ge(S["pre_ready"], T)
                    if start and g:
                        pe.wait_ge(S["w_ready"], b + 1)
                    ins = bank_step(b, jt, u, start)
                ins.then_inc(S["pe_group"], 1)

            pe.wait_ge(S["hT_ready"], T)
            for g in range(2):
                n, first, second = T * g, HALF * g, HALF * (1 - g)
                for u in range(AR):
                    s_step(first + u, n + u, u, u == 0, g)
                with pe.Fori(1, HALF // AR) as p:
                    for u in range(AR):
                        s_step(AR * p + (first + u), AR * p + (n + u), u)
                n += HALF
                with pe.Fori(0, HALF // AR - 1) as p:
                    for u in range(AR):
                        s_step(AR * p + (second + u), AR * p + (n + u), u)
                n += HALF - AR
                last = second + HALF - AR
                for u in range(AR - 2):
                    s_step(last + u, n + u, u)
                pe.wait_ge(S["t_ready"], last + AR)
                pe.wait_ge(S["s_ready"], n + AR)
                for b in range(HALF):
                    for u in range(AR - 2, AR):
                        ins = bank_step(b, last + u, u, False)
                    ins.then_inc(S["bank_done"], 1)

            def y_tile(i, u, reused):
                if reused is not None:
                    pe.wait_ge(S["y_used"], reused)
                for j in range(T):
                    if type(i) is int and i == 0:
                        pe.wait_ge(S["w_ready"], j + 1)
                    for s in range(2):
                        ins = pe.matmul(psum[:, u, :], adjT[:, j, bass.ts(i, P)], w_split[:, s, j, :],
                                        start=j == 0 and s == 0, stop=j == T - 1 and s == 1)
                ins.then_inc(S["y_ready"], 1)

            pe.wait_ge(S["w_ready"], HALF + 2)
            y_tile(0, 0, None)
            y_tile(1, 1, None)
            with pe.Fori(1, T // 2) as p:
                for u in range(2):
                    y_tile(2 * p + u, u, 2 * p + u - 1)


_INS = ["x", "adj", "L0_gnn_W_seq", "L0_gnn_a1", "L0_gnn_a2", "L0_gnn_W_out", "L0_gnn_b_out"]


def kernel(**inputs):
    import numpy as _np
    import concourse.bacc as _bacc
    from concourse import mybir as _mybir
    from concourse.bass_utils import run_bass_kernel_spmd as _run

    nc = _bacc.Bacc("TRN2", target_bir_lowering=False, num_devices=1)
    arrays, args = {}, []
    for name in _INS:
        a = _np.ascontiguousarray(inputs[name])
        arrays[f"in_{name}_dram"] = a
        args.append(nc.dram_tensor(f"in_{name}_dram", a.shape, _mybir.dt.from_np(a.dtype), kind="ExternalInput").ap())
    args.append(nc.dram_tensor("out_0_dram", (N, D), F32, kind="ExternalOutput").ap())
    gat_gcn_kernel(nc, *args)
    r = _run(nc, [arrays], core_ids=[0])
    return r.results[0]["out_0_dram"]
```
